# Optimizing a Trainium2 kernel written in Bass

```python
import numpy as np
import jax
import jax.numpy as jnp

def _softmax(x, axis=-1):
    return jax.nn.softmax(x, axis=axis)

def _gelu(x):
    return jax.nn.gelu(x, approximate=True)

def _silu(x):
    return jax.nn.silu(x)

def _sigmoid(x):
    return jax.nn.sigmoid(x)

def _layernorm(x, axis=-1, eps=1e-05):
    m = jnp.mean(x, axis=axis, keepdims=True)
    v = jnp.var(x, axis=axis, keepdims=True)
    return (x - m) / jnp.sqrt(v + eps)

def _scatter_add(tgt, idx, src, axis=0):
    return tgt.at[idx].add(src)

def _segment_sum(src, seg, n):
    return jax.ops.segment_sum(src, seg, n)
kernel_name = 'mk_gps_d1_gnn_r8_bc45b9'

def setup_inputs(seed: int=0):
    np.random.seed(seed)
    _w = jnp.asarray

    def _rec_inputs():
        import jax
        import jax.numpy as jnp
        _gk = jax.random.key(seed)
        x = -0.0003713 + 1 * jax.random.normal(jax.random.fold_in(_gk, 1), (6250, 256), jnp.float32)
        _s = jax.random.randint(jax.random.fold_in(_gk, 2), (50000,), 0, 6250, jnp.int32)
        _d = jax.random.randint(jax.random.fold_in(_gk, 3), (50000,), 0, 6250, jnp.int32)
        _loop = jnp.arange(6250, dtype=jnp.int32)
        src = jnp.concatenate([_s, _d, _loop])
        dst = jnp.concatenate([_d, _s, _loop])
        _o = jnp.argsort(dst, stable=True)
        src = src[_o]
        dst = dst[_o]
        edge_weight = jax.random.uniform(jax.random.fold_in(_gk, 12), (106250,), jnp.float32, 0.0, 999998)
        node_vec = jax.random.uniform(jax.random.fold_in(_gk, 13), (6250,), jnp.float32, 0.0, 999884)
        return (x, src, dst, edge_weight, node_vec)
    x, src, dst, edge_weight, node_vec = _rec_inputs()

    def _L0_gnn_setup():
        import jax, jax.numpy as jnp
        import numpy as np
        NUM_NODES = 6250
        NUM_EDGES = 100000
        INPUT_DIM = 256
        OUTPUT_DIM = 256
        NUM_HEADS = 8
        HEAD_DIM = OUTPUT_DIM // NUM_HEADS
        key = jax.random.key(seed)
        ks = jax.random.split(key, 14)
        x = jax.random.normal(ks[0], (NUM_NODES, INPUT_DIM), dtype=jnp.float32)
        edge_index = jax.random.randint(ks[1], (2, NUM_EDGES), 0, NUM_NODES, dtype=jnp.int32)
        edge_time = jax.random.uniform(ks[2], (NUM_EDGES,), dtype=jnp.float32) * 1000000.0
        node_time = jax.random.uniform(ks[3], (NUM_NODES,), dtype=jnp.float32) * 1000000.0
        s_in = 1.0 / np.sqrt(INPUT_DIM)
        s_out = 1.0 / np.sqrt(OUTPUT_DIM)
        s_t = 1.0 / np.sqrt(2.0)
        Wq = jax.random.uniform(ks[4], (INPUT_DIM, OUTPUT_DIM), jnp.float32, -s_in, s_in)
        bq = jax.random.uniform(ks[5], (OUTPUT_DIM,), jnp.float32, -s_in, s_in)
        Wk = jax.random.uniform(ks[6], (INPUT_DIM, OUTPUT_DIM), jnp.float32, -s_in, s_in)
        bk = jax.random.uniform(ks[7], (OUTPUT_DIM,), jnp.float32, -s_in, s_in)
        Wv = jax.random.uniform(ks[8], (INPUT_DIM, OUTPUT_DIM), jnp.float32, -s_in, s_in)
        bv = jax.random.uniform(ks[9], (OUTPUT_DIM,), jnp.float32, -s_in, s_in)
        Wt = jax.random.uniform(ks[10], (2, NUM_HEADS), jnp.float32, -s_t, s_t)
        bt = jax.random.uniform(ks[11], (NUM_HEADS,), jnp.float32, -s_t, s_t)
        Wo = jax.random.uniform(ks[12], (OUTPUT_DIM, OUTPUT_DIM), jnp.float32, -s_out, s_out)
        bo = jax.random.uniform(ks[13], (OUTPUT_DIM,), jnp.float32, -s_out, s_out)
        return {'x': x, 'edge_index': edge_index, 'edge_time': edge_time, 'node_time': node_time, 'Wq': Wq, 'bq': bq, 'Wk': Wk, 'bk': bk, 'Wv': Wv, 'bv': bv, 'Wt': Wt, 'bt': bt, 'Wo': Wo, 'bo': bo}
    _L0_gnn_all = _L0_gnn_setup()
    _L0_gnn_in = {k: v for k, v in _L0_gnn_all.items() if k in ('Wq', 'bq', 'Wk', 'bk', 'Wv', 'bv', 'Wt', 'bt', 'Wo', 'bo')}
    del _L0_gnn_all

    def _L0_mix_setup():
        import jax, jax.numpy as jnp
        import numpy as np
        HEADS = 8
        EPS = 1e-05

        def _ln(t, w, b, headc):
            m = jnp.mean(t, axis=-1, keepdims=True)
            d = t - m
            std = jnp.sqrt(jnp.sum(d * d, axis=-1, keepdims=True) / (headc - 1))
            return w * (d / (std + EPS)) + b
        key = jax.random.key(seed)
        B, N, C = (32, 512, 256)
        headc = C // HEADS
        x = jax.random.normal(key, (B, N, C), dtype=jnp.float32)
        return {'x': x, 'kln_weight': jnp.ones((HEADS, 1, headc), dtype=jnp.float32), 'kln_bias': jnp.zeros((HEADS, 1, headc), dtype=jnp.float32), 'vln_weight': jnp.ones((HEADS, 1, headc), dtype=jnp.float32), 'vln_bias': jnp.zeros((HEADS, 1, headc), dtype=jnp.float32)}
    _L0_mix_all = _L0_mix_setup()
    _L0_mix_in = {k: v for k, v in _L0_mix_all.items() if k in ('kln_weight', 'kln_bias', 'vln_weight', 'vln_bias')}
    del _L0_mix_all

    def _L0_ffn_setup():
        import jax, jax.numpy as jnp
        import numpy as np
        B, S, D, H, E, K = (8, 1024, 256, 1024, 8, 2)
        key = jax.random.key(seed)
        ks = jax.random.split(key, 7)
        s_in = 1.0 / np.sqrt(D)
        s_hid = 1.0 / np.sqrt(H)
        return {'x': jax.random.normal(ks[0], (B, S, D), dtype=jnp.float32), 'Wg': jax.random.uniform(ks[1], (E, D), jnp.float32, -s_in, s_in), 'bg': jax.random.uniform(ks[2], (E,), jnp.float32, -s_in, s_in), 'W1': jax.random.uniform(ks[3], (E, H, D), jnp.float32, -s_in, s_in), 'b1': jax.random.uniform(ks[4], (E, H), jnp.float32, -s_in, s_in), 'W2': jax.random.uniform(ks[5], (E, D, H), jnp.float32, -s_hid, s_hid), 'b2': jax.random.uniform(ks[6], (E, D), jnp.float32, -s_hid, s_hid)}
    _L0_ffn_all = _L0_ffn_setup()
    _L0_ffn_in = {k: v for k, v in _L0_ffn_all.items() if k in ('Wg', 'bg', 'W1', 'b1', 'W2', 'b2')}
    del _L0_ffn_all
    return {'x': x, 'src': src, 'dst': dst, 'edge_weight': edge_weight, 'node_vec': node_vec, 'L0_gnn_Wq': _L0_gnn_in['Wq'], 'L0_gnn_bq': _L0_gnn_in['bq'], 'L0_gnn_Wk': _L0_gnn_in['Wk'], 'L0_gnn_bk': _L0_gnn_in['bk'], 'L0_gnn_Wv': _L0_gnn_in['Wv'], 'L0_gnn_bv': _L0_gnn_in['bv'], 'L0_gnn_Wt': _L0_gnn_in['Wt'], 'L0_gnn_bt': _L0_gnn_in['bt'], 'L0_gnn_Wo': _L0_gnn_in['Wo'], 'L0_gnn_bo': _L0_gnn_in['bo'], 'L0_mix_kln_weight': _L0_mix_in['kln_weight'], 'L0_mix_kln_bias': _L0_mix_in['kln_bias'], 'L0_mix_vln_weight': _L0_mix_in['vln_weight'], 'L0_mix_vln_bias': _L0_mix_in['vln_bias'], 'L0_ffn_Wg': _L0_ffn_in['Wg'], 'L0_ffn_bg': _L0_ffn_in['bg'], 'L0_ffn_W1': _L0_ffn_in['W1'], 'L0_ffn_b1': _L0_ffn_in['b1'], 'L0_ffn_W2': _L0_ffn_in['W2'], 'L0_ffn_b2': _L0_ffn_in['b2']}

def reference(x, src, dst, edge_weight, node_vec, L0_gnn_Wq, L0_gnn_bq, L0_gnn_Wk, L0_gnn_bk, L0_gnn_Wv, L0_gnn_bv, L0_gnn_Wt, L0_gnn_bt, L0_gnn_Wo, L0_gnn_bo, L0_mix_kln_weight, L0_mix_kln_bias, L0_mix_vln_weight, L0_mix_vln_bias, L0_ffn_Wg, L0_ffn_bg, L0_ffn_W1, L0_ffn_b1, L0_ffn_W2, L0_ffn_b2):
    import jax
    import jax.numpy as jnp

    def _L0_gnn_ref(x, edge_index, edge_time, node_time, Wq, bq, Wk, bk, Wv, bv, Wt, bt, Wo, bo):
        import jax, jax.numpy as jnp
        import numpy as np
        NUM_NODES = 6250
        NUM_EDGES = 100000
        INPUT_DIM = 256
        OUTPUT_DIM = 256
        NUM_HEADS = 8
        HEAD_DIM = OUTPUT_DIM // NUM_HEADS
        n = x.shape[0]
        q = (x @ Wq + bq).reshape(n, NUM_HEADS, HEAD_DIM)
        k = (x @ Wk + bk).reshape(n, NUM_HEADS, HEAD_DIM)
        v = (x @ Wv + bv).reshape(n, NUM_HEADS, HEAD_DIM)
        src, dst = (edge_index[0], edge_index[1])
        time_diff = edge_time - node_time[dst]
        time_features = jnp.stack([jnp.sign(time_diff), jnp.log1p(jnp.abs(time_diff) / 3600.0)], axis=-1)
        temporal_weights = time_features @ Wt + bt
        scale = HEAD_DIM ** (-0.5)
        scores = jnp.einsum('ehd,ehd->eh', q[dst], k[src]) * scale + temporal_weights
        alpha = jax.nn.softmax(scores, axis=0)
        msg = alpha[..., None] * v[src]
        out = jax.ops.segment_sum(msg, dst, num_segments=n)
        out = out.reshape(n, OUTPUT_DIM)
        return out @ Wo + bo

    def _L0_mix_ref(x, kln_weight, kln_bias, vln_weight, vln_bias):
        import jax, jax.numpy as jnp
        import numpy as np
        HEADS = 8
        EPS = 1e-05

        def _ln(t, w, b, headc):
            m = jnp.mean(t, axis=-1, keepdims=True)
            d = t - m
            std = jnp.sqrt(jnp.sum(d * d, axis=-1, keepdims=True) / (headc - 1))
            return w * (d / (std + EPS)) + b
        B, N, C = x.shape
        headc = C // HEADS
        qkv = x.reshape(B, N, HEADS, headc).transpose(0, 2, 1, 3)
        k = _ln(qkv, kln_weight, kln_bias, headc)
        v = _ln(qkv, vln_weight, vln_bias, headc)
        kv = jnp.einsum('bhnd,bhne->bhde', k, v) / N
        out = jnp.einsum('bhnd,bhde->bhne', qkv, kv)
        out = out.transpose(0, 2, 1, 3).reshape(B, N, C)
        return out + x

    def _L0_ffn_ref(x, Wg, bg, W1, b1, W2, b2):
        import jax, jax.numpy as jnp
        import numpy as np
        B, S, D, H, E, K = (8, 1024, 256, 1024, 8, 2)
        gate_scores = jnp.einsum('bsd,ed->bse', x, Wg) + bg
        topk_scores, topk_idx = jax.lax.top_k(gate_scores, K)
        topk_probs = jax.nn.softmax(topk_scores, axis=-1)
        combine = jnp.sum(topk_probs[..., None] * jax.nn.one_hot(topk_idx, E, dtype=x.dtype), axis=-2)
        out = jnp.zeros_like(x)
        for e in range(E):
            h = jax.nn.relu(jnp.einsum('bsd,hd->bsh', x, W1[e]) + b1[e])
            y = jnp.einsum('bsh,dh->bsd', h, W2[e]) + b2[e]
            out = out + combine[..., e:e + 1] * y
        return out
    edge_index = jnp.stack([src, dst])
    xn = _layernorm(x, axis=-1)
    x = x + _L0_gnn_ref(xn, edge_index, edge_weight, node_vec, L0_gnn_Wq, L0_gnn_bq, L0_gnn_Wk, L0_gnn_bk, L0_gnn_Wv, L0_gnn_bv, L0_gnn_Wt, L0_gnn_bt, L0_gnn_Wo, L0_gnn_bo) + _L0_mix_ref(xn[None], L0_mix_kln_weight, L0_mix_kln_bias, L0_mix_vln_weight, L0_mix_vln_bias)[0]
    x = x + _L0_ffn_ref(_layernorm(x, axis=-1)[None], L0_ffn_Wg, L0_ffn_bg, L0_ffn_W1, L0_ffn_b1, L0_ffn_W2, L0_ffn_b2)[0]
    return x

_drawn_inputs = setup_inputs


def setup_inputs(seed=0):
    import zlib

    import numpy as np

    out = dict(_drawn_inputs(seed))
    spreads = {'L0_mix_kln_weight': (1.0, 0.2),
     'L0_mix_kln_bias': (0.0, 0.444),
     'L0_mix_vln_weight': (1.0, 0.2),
     'L0_mix_vln_bias': (0.0, 0.445)}
    factors = {'edge_weight': 35.437,
     'node_vec': 25.52,
     'L0_gnn_Wq': 8.0,
     'L0_gnn_bq': 8.0,
     'L0_gnn_Wk': 8.0,
     'L0_gnn_bk': 8.0,
     'L0_gnn_Wv': 8.0,
     'L0_gnn_bv': 64.0,
     'L0_gnn_Wt': 8.0,
     'L0_gnn_Wo': 8.0,
     'L0_gnn_bo': 4.113,
     'L0_ffn_bg': 5.068,
     'L0_ffn_b1': 8.0,
     'L0_ffn_b2': 8.0,
     'L0_gnn_bt': 64.0}
    for name, (base, spread) in spreads.items():
        noise = np.random.default_rng([zlib.crc32(name.encode()), seed]).standard_normal(out[name].shape)
        drawn = base * np.exp(spread * noise) if base else spread * noise
        out[name] = jnp.asarray(drawn.astype(out[name].dtype))
    for name, factor in factors.items():
        out[name] = (out[name] * factor).astype(out[name].dtype)
    return out
```

```python
from contextlib import ExitStack

import concourse.bass as bass
from concourse import mybir

F32 = mybir.dt.float32
BF16 = mybir.dt.bfloat16
I32 = mybir.dt.int32
ALU = mybir.AluOpType
ACT = mybir.ActivationFunctionType
X = mybir.AxisListType.X

P = 128
N = 6250
D = 256
H = 8
HD = D // H
NB = -(-N // P)
NPAD = NB * P
E = 106250
TC = 4
CH = TC * P
NC = -(-E // CH)
GC = 4
GT = GC * TC
NG = NC // GC
EPAD = NC * CH
NX = 8
F = 1024
FC = F // P
NT = (2 * NPAD + NX * (P - 1)) // P
LN_EPS = 1e-5
NEG = -1.0e30
QSCALE = HD ** -0.5
STAGE = 9
assert NC % GC == 0 and NG % 2 == 0


class Count:

    def __init__(self, sem):
        self.sem, self.base, self.n = sem, 0, 0

    def at(self, base):
        self.base, self.n = base, 0
        return self

    def inc(self, ins):
        ins.then_inc(self.sem, 1)
        self.n += 1

    def wait(self, eng):
        eng.wait_ge(self.sem, self.base + self.n)


def pairs(eng, n, body, peel=2):
    for i in range(peel):
        body(i, i % 2)
    i = peel
    turns = (n - i) // 2
    if turns:
        with eng.Fori(0, turns) as t:
            body(t * 2 + i, 0)
            body(t * 2 + (i + 1), 1)
    if (n - i) % 2:
        body(n - 1, (n - 1) % 2)


def build(nc, a, out):
    ctx = ExitStack()
    with ctx:
        def sb(name, shape, dt=F32):
            return ctx.enter_context(nc.sbuf_tensor(name, shape, dt))

        def sem(name):
            return ctx.enter_context(nc.semaphore(name))

        def dram(name, shape, dt=F32):
            return nc.dram_tensor(name, shape, dt, kind="Internal").ap()

        kv_d = dram("kv_rows", [NPAD, 2 * D])
        xs_d = dram("expert_rows_in", [NT * P, D])
        ys_d = dram("expert_rows_out", [NT * P, D])
        x2_d = dram("residual_rows", [NPAD, D])
        xnT_d = dram("xn_transposed", [NPAD, D])
        span_d = dram("chunk_spans", [3, NC])

        R1 = sb("R1", [P, NB * D])
        x_sb = R1[:, :].rearrange("p (i d) -> p i d", d=D)
        acc = R1[:, :].rearrange("p (i k n) -> p i k n", k=2, n=P)
        QW = NB * 3 * D // 2
        KVW = 2 * GC * TC * 2 * D
        R2 = sb("R2", [P, QW + KVW])
        q3 = R2[:, 0:QW].bitcast(BF16).rearrange("p (i j d) -> p i j d", j=3, d=D)
        ring = R2[:, QW:QW + KVW].rearrange("p (s t d) -> p s t d", s=2 * GC, t=TC)
        used = [QW]

        def work(shape):
            n = 1
            for s in shape:
                n *= s
            v = R2[:, used[0]:used[0] + n]
            used[0] += n
            if len(shape) == 2:
                v = v.rearrange("p (a b) -> p a b", b=shape[1])
            if len(shape) == 3:
                v = v.rearrange("p (a b c) -> p a b c", b=shape[1], c=shape[2])
            return v

        xn = work((2, D))
        zb = work((2, 2, P + 4))
        xnT = work((2, D))
        kvs = work((2, 2 * D))
        qf = work((2, D))
        qr = work((2, D))
        sq = work((2, D))
        wkv = work((2, 2 * D))
        wq = work((2, D))
        bkv = work((2 * D,))
        bqs = work((D,))
        dch = work((2, CH)).bitcast(I32)
        bnst = work((NB, 6))
        vwb = work((2 * D,))
        nvf = work((NB,))
        nvr = work((NB,))
        small = work((2, 8 * 4))
        zrow = work((D,))
        zzs = work((2, P + 4))
        zsq = work((2, P))
        mt = work((3, P))
        hmask = work((P,))
        tabf = work((6, NC))[0:1, :, :]
        assert used[0] <= QW + KVW

        nv3 = sb("nv3", [P, NB, 4], BF16)
        mv = sb("mv", [P, NB, 2])
        rs = sb("rs", [P, 4, NB])
        ident = sb("ident", [P, P])
        ident16 = sb("ident16", [P, P], BF16)
        iota16 = sb("iota16", [P, P], BF16)
        ones = sb("ones", [P, P])
        zero16 = sb("zero16", [1, CH], BF16)
        headind = sb("headind", [H, 2, P])
        blk0 = sb("blk0", [P, NB])
        bd = sb("bd", [P, 2, P])
        kwb = sb("kwb", [P, 4])
        wtb = sb("wtb", [P, 3, H])
        tab = sb("tab", [1, NC, 4], I32)
        spf = sb("spf", [NC // 2, 3, 2])
        spi = sb("spi", [NC // 2, 2, 2], I32)

        ps = ctx.enter_context(nc.psum_tensor("ps", [P, 8, 512], F32))
        zz_ps = ps[:, 6, 0:2 * (P + 4)].rearrange("p (k c) -> p k c", k=2)

        b1 = sb("b1", [P, NX, FC])
        cT = sb("cT", [NX, 2, P])
        pos = sb("pos", [P, NB, 2], I32)
        place = sb("place", [P, 2, 2], I32)
        pw = sb("pw", [P, 2, NB])
        etab = sb("etab", [1, P], I32)

        src = sb("src", [P, 2, GT], I32)
        dst = sb("dst", [P, 2, GT], I32)
        ew = sb("ew", [P, 2, GT])
        dstB = sb("dstB", [P, GT])
        locA = sb("locA", [P, 2, TC])
        locB = sb("locB", [P, 2, TC])
        S16 = sb("S16", [P, TC, P], BF16)
        ST = sb("ST", [P, TC, P], BF16)
        S32 = sb("S32", [P, TC, P])
        sc = sb("sc", [P, GT, H])
        prob = sb("prob", [P, GT, H])
        nvs = sb("nvs", [P, GT, 3])
        tf = sb("tf", [P, 6, GT])
        tw = sb("tw", [P, 2, GT, H])
        mxp = sb("mxp", [P, H])
        m8 = sb("m8", [H, 1])
        dg = sb("dg", [H, H])
        Mn = sb("Mn", [P, 2, H + 2])
        Mblk = sb("Mblk", [P, NB, 2])
        fd = sb("fd", [P, 2])
        fe = sb("fe", [P, 2])
        fz = sb("fz", [P, 2, H])
        Zp = sb("Zp", [P, 2, H])
        zsum = sb("zsum", [P, H])
        z8 = sb("z8", [H, 2])
        G = sb("G", [P, NB, 2])

        NWL = 17 * 16
        s_w = sem("weights_in")
        s_x = [sem(f"x_in{j}") for j in range(7)]
        s_c = sem("constants")
        s_v = sem("dve_line")
        s_l1 = sem("dve_line_stage1")
        s_var = sem("variances_plus_eps")
        s_std = sem("deviations")
        s_xn = sem("xn_ready")
        s_d = sem("head_centred")
        s_z = sem("z_ready")
        s_ss = sem("square_sums")
        s_tr = sem("xn_turned")
        s_xt = sem("xnT_copied")
        s_sq = sem("squares")
        s_rt = sem("roots")
        s_kvp = sem("qkv_products")
        s_kve = sem("kv_rows_ready")
        s_qe = sem("q_ready")
        s_q1 = sem("q_part1")
        s_q2 = sem("q_part2")
        s_r1 = sem("q_rest")
        s_r2 = sem("q_part3")
        s_zz = sem("z_products")
        s_st = [sem(f"rows_stored{j}") for j in range(2)]
        s_mix = sem("mix_line")
        s_spd = sem("spans_ready")
        s_sp = sem("spans_moved")
        s_tab = sem("table_ready")
        s_mxp = sem("z_sums_as_row")
        s_bd = sem("mix_matrix_ready")
        s_az = sem("acc_zeroed")

        s_in = [sem(f"edges_in{j}") for j in range(2)]
        s_g = [sem(f"rows_gathered{j}") for j in range(2 * GC)]
        s_la = sem("dve_line_spread_visit")
        s_lb = sem("dve_line_sum_visit")
        s_lp = sem("dve_line_scores")
        s_lm = sem("dve_line_group")
        s_S16 = sem("onehot16_ready")
        s_T = sem("onehot_turned")
        s_ST = sem("onehotT_copied")
        s_Q = sem("q_spread")
        s_pq = sem("spread_q_read")
        s_msg = sem("values_weighted")
        s_fd = sem("max_step_ready")
        s_f = sem("rescale_ready")
        s_S32 = sem("onehot32_ready")
        s_O = sem("node_sums_ready")
        s_acc = sem("node_sums_added")
        s_abs = sem("time_gap_ready")
        s_ln = sem("log_ready")
        s_mx = sem("partition_max_ready")
        s_mt = sem("max_turned")
        s_m8 = sem("head_max_ready")
        s_mb = sem("max_spread")
        s_sh = sem("scores_shifted")
        s_pe = sem("probs_ready")
        s_grp = sem("group_done")
        s_zl = sem("dve_line_sumexp")
        s_fin = sem("final_line")
        s_grp0 = sem("group_state_set")
        s_fz = sem("sum_rescale_ready")
        s_w3 = sem("stage3_weights")
        s_G = sem("final_scales_ready")
        s_fp = sem("final_products")
        s_fa = sem("final_exps")

        s_in3 = [sem(f"stage3_in{j}") for j in range(2)]
        s_xb = sem("x_plus_bias")
        s_as = sem("acc_scaled")
        s_p3 = sem("x2_products")
        s_x2 = sem("x2_ready")
        s_cs = sem("combine_copied_out")
        s_x2b = sem("residual_with_bias")
        s_we = sem("expert_weights_in")
        s_posx = sem("row_to_scatter")
        s_pl = sem("places_copied")
        s_o = sem("output_ready")
        s_ft = sem("rows_turned3")
        s_gp = sem("gate_products")
        s_fc = sem("turned3_copied")
        s_dm = sem("gate_gap")
        s_em = sem("gate_exp")
        s_ct = sem("combine_turned")
        s_bp = sem("bias_products")
        s_cc = sem("combine_copied")
        s_y = sem("second_layer_done")
        s_ha = sem("hidden_low_ready")
        s_hd = sem("hidden_high_ready")
        s_xf = sem("rows_normalised3")
        s_g2 = sem("gates_ready")
        s_oh = sem("choice_ready")
        s_cnt = sem("choice_counts")
        s_comb = sem("combine_ready")
        s_xc = sem("turned4_copied")
        s_xt4 = sem("rows_turned4")
        s_etab = sem("tile_experts_ready")
        s_yc = sem("result_copied")
        s_bn = sem("stats3")
        s_v3 = sem("dve_line3")
        s_xz = sem("xs_zeroed")
        s_o1 = sem("first_expert_added")
        s_w1 = [sem(f"first_layer_weights_in{j}") for j in range(2)]
        s_x2s = [sem(f"residual_stored{j}") for j in range(2)]
        s_sc = [sem(f"rows_scattered{j}") for j in range(2)]
        s_yst = [sem(f"result_stored{j}") for j in range(2)]
        s_yg = [sem(f"expert_rows_in{j}") for j in range(2)]
        s_h1 = [sem(f"first_layer_done{j}") for j in range(2)]
        s_xs = [sem(f"expert_tile_in{j}") for j in range(2)]
        s_x5 = [sem(f"residual_in{j}") for j in range(2)]
        s_out5 = [sem(f"output_stored{j}") for j in range(2)]
        block = ctx.enter_context(nc.Block())

        def flat(ap):
            return ap.rearrange("p a d -> p (a d)")

        def blk(t, i):
            return flat(t[:, bass.ds(i, 1), :])

        def q_part(i, j):
            return flat(q3[:, bass.ds(i, 1), j, :])

        def sync1(sp):
            sp.dma_start(ident[:, :], a["ident"]).then_inc(s_w, 16)
            for j in range(7):
                sp.dma_start(x_sb[:, 7 * j:7 * j + 7, :],
                             a["x"][7 * j * P:(7 * j + 7) * P, :].rearrange("(i p) d -> p i d", p=P)).then_inc(s_x[j], 16)
            loads = ((wkv[:, :, 0:D], a["wk"].rearrange("(k p) n -> p k n", p=P)),
                     (wkv[:, :, D:2 * D], a["wv"].rearrange("(k p) n -> p k n", p=P)),
                     (wq, a["wq"].rearrange("(k p) n -> p k n", p=P)),
                     (bkv[:, 0:D], a["bk"].partition_broadcast(P)),
                     (bkv[:, D:2 * D], a["bv"].partition_broadcast(P)),
                     (bqs, a["bq"].partition_broadcast(P)),
                     (vwb[:, 0:D], a["vlw"].partition_broadcast(P)),
                     (vwb[:, D:2 * D], a["vlb"].partition_broadcast(P)),
                     (kwb[:, 0:2], a["klw"]),
                     (kwb[:, 2:4], a["klb"]),
                     (wtb[:, 0:2, :].rearrange("p a h -> p (a h)"), a["wt"].partition_broadcast(P)),
                     (wtb[:, 2, :], a["bt"].partition_broadcast(P)),
                     (nvf, a["nv"]),
                     (headind[:, :, :], a["headind"]),
                     (hmask, a["hmask"]),
                     (dch[0:NC // 2, :, :], a["dst_rows"]))
            assert NWL == 16 * (len(loads) + 1)
            for d, s in loads:
                sp.dma_start(d, s).then_inc(s_w, 16)
            sp.wait_ge(s_c, NCONST)
            sp.dma_start(xs_d.rearrange("(j p) d -> p j d", p=P), zrow.unsqueeze(1).to_broadcast([P, NT, D])).then_inc(s_xz, 16)
            sp.wait_ge(s_spd, 1)
            for j in range(3):
                sp.dma_start(span_d[j, :].rearrange("(p two) -> p two", two=2), spf[:, j, :]).then_inc(s_sp, 16)
            sp.wait_ge(s_sp, 48)
            sp.dma_start(tabf[0:1, 0:3, :], span_d.unsqueeze(0)).then_inc(s_sp, 16)

            def store(i, slot):
                sp.wait_ge(s_xt, i + 1)
                sp.dma_start(xnT_d[bass.ds(i * P, P), :], xnT[:, slot, :]).then_inc(s_st[slot], 16)
                sp.wait_ge(s_kve, i + 1)
                sp.dma_start(kv_d[bass.ds(i * P, P), :], kvs[:, slot, :]).then_inc(s_st[slot], 16)
            pairs(sp, NB, store, 0)

        NCONST = 8

        def pool1(pool):
            g = Count(s_c)
            g.inc(pool.memset(ones[:, :], 1.0))
            g.inc(pool.memset(zero16[:, :], 0.0))
            g.inc(pool.memset(zb[:, :, :, P:P + 4], 1.0))
            g.inc(pool.iota(iota16[:, :], [[1, P]], channel_multiplier=0, allow_small_or_imprecise_dtypes=True))
            g.inc(pool.iota(blk0[:, :], [[P, NB]], channel_multiplier=0, allow_small_or_imprecise_dtypes=True))
            g.inc(pool.memset(zrow, 0.0))
            g.inc(pool.memset(Mblk[:, :, :], NEG))
            pool.wait_ge(s_w, NWL)
            g.inc(pool.tensor_copy(ident16[:, :], ident[:, :]))

            def split(i, slot):
                if isinstance(i, int) and i == 0:
                    pool.wait_ge(s_c, NCONST)
                pool.wait_ge(s_q1, i + 1)
                pool.tensor_tensor(qr[:, slot, :], qf[:, slot, :], q_part(i, 0), ALU.subtract).then_inc(s_r1, 1)
                pool.tensor_copy(blk(x_sb, i), zrow).then_inc(s_az, 1)
                pool.wait_ge(s_q2, i + 1)
                pool.tensor_tensor(q_part(i, 2), qr[:, slot, :], q_part(i, 1), ALU.subtract).then_inc(s_r2, 1)
            pairs(pool, NB, split)

        def rstd(v, c):
            c.inc(v.reciprocal(rs[:, 2, :], rs[:, 1, :]))
            c.wait(v)
            c.inc(v.tensor_tensor(rs[:, 3, :], rs[:, 2, :], rs[:, 2, :], ALU.mult))
            c.wait(v)
            c.inc(v.tensor_tensor(rs[:, 3, :], rs[:, 3, :], rs[:, 0, :], ALU.mult))
            c.wait(v)
            c.inc(v.tensor_scalar(rs[:, 3, :], rs[:, 3, :], -0.5, 1.5, ALU.mult, ALU.add))
            c.wait(v)
            c.inc(v.tensor_tensor(rs[:, 2, :], rs[:, 2, :], rs[:, 3, :], ALU.mult))
            c.wait(v)

        def dve1(v):
            c = Count(s_v)
            v.wait_ge(s_w, NWL)
            c.inc(v.tensor_scalar(bqs, bqs, QSCALE, None, ALU.mult))
            c.inc(v.tensor_copy(nv3[:, :, 0], nvf))
            c.inc(v.tensor_scalar(wtb[:, 0, :], wtb[:, 0, :], -1.0, None, ALU.mult))
            for j in range(7):
                v.wait_ge(s_x[j], 16)
                for i in range(7 * j, 7 * j + 7):
                    c.inc(v.bn_stats(bnst[:, i, :], x_sb[:, i, :]))
            c.wait(v)
            for i in range(NB):
                c.inc(v.bn_aggr(mv[:, i, :], bnst[:, i, :]))
            c.wait(v)
            v.tensor_scalar(rs[:, 0, :], mv[:, :, 1], LN_EPS, None, ALU.add).then_inc(s_var, 1)
            v.wait_ge(s_std, 1)
            rstd(v, c)
            c.inc(v.tensor_tensor(nvr, nvf, nv3[:, :, 0], ALU.subtract))
            c.wait(v)
            c.inc(v.tensor_copy(nv3[:, :, 1], nvr))
            c.wait(v)
            c.inc(v.tensor_tensor(nv3[:, :, 2], nvr, nv3[:, :, 1], ALU.subtract))
            rows = slice(0, NC // 2)
            c.inc(v.tensor_reduce(spf[:, 0, :], dch[rows, :, :], X, ALU.min))
            c.inc(v.tensor_reduce(spf[:, 1, :], dch[rows, :, :], X, ALU.max))
            c.wait(v)
            c.inc(v.tensor_copy(spi[:, :, :], spf[:, 0:2, :]))
            c.wait(v)
            c.inc(v.tensor_scalar(spi[:, :, :], spi[:, :, :], 7, None, ALU.logical_shift_right))
            c.wait(v)
            c.inc(v.tensor_copy(spf[:, 0:2, :], spi[:, :, :]))
            c.wait(v)
            c.inc(v.tensor_scalar(spf[:, 0:2, :], spf[:, 0:2, :], float(NB - 1), None, ALU.min))
            c.wait(v)
            c.inc(v.tensor_scalar(spf[:, 1, :], spf[:, 1, :], 1.0, None, ALU.add))
            c.wait(v)
            v.tensor_tensor(spf[:, 2, :], spf[:, 1, :], spf[:, 0, :], ALU.subtract).then_inc(s_spd, 1)
            v.wait_ge(s_sp, 64)
            v.wait_ge(s_c, NCONST)
            c.inc(v.memset(tabf[:, 3, :], 1.0))
            c.wait(v)
            c.inc(v.tensor_tensor_scan(tabf[:, 4, :], tabf[:, 3, :], tabf[:, 2, :], 0.0, ALU.mult, ALU.add))
            c.wait(v)
            c.inc(v.tensor_tensor(tabf[:, 5, :], tabf[:, 4, :], tabf[:, 2, :], ALU.subtract))
            c.wait(v)
            v.tensor_copy(tab[:, :, 0], tabf[:, 0, :]).then_inc(s_tab, 1)
            v.tensor_copy(tab[:, :, 1], tabf[:, 2, :]).then_inc(s_tab, 1)
            v.tensor_copy(tab[:, :, 2], tabf[:, 5, :]).then_inc(s_tab, 1)
            v.tensor_copy(tab[:, :, 3], tabf[:, 4, :]).then_inc(s_tab, 1)

            h = Count(s_l1)

            def sm(slot):
                return small[:, slot, :].rearrange("p (a h) -> p a h", h=H)

            def heads(t):
                return t.rearrange("p k (h d) -> p k h d", d=HD)

            def per_head(t):
                return t.rearrange("p (k h) -> p k h", k=2).unsqueeze(3).to_broadcast([P, 2, H // 2, HD])

            def normal(i, slot):
                xo = xn[:, slot, :]
                warm = not isinstance(i, int) or i >= 2
                if warm:
                    v.wait_ge(s_tr, i - 1)
                v.tensor_scalar(xo, blk(x_sb, i), flat(mv[:, bass.ds(i, 1), 0:1]), rs[:, 2, bass.ds(i, 1)],
                                ALU.subtract, ALU.mult).then_inc(s_xn, 1)
                v.wait_ge(s_xn, i + 1)
                h.inc(v.tensor_reduce(sm(slot)[:, 0, :], xo.rearrange("p (h d) -> p h d", d=HD), X, ALU.add))
                h.wait(v)
                h.inc(v.tensor_scalar(sm(slot)[:, 1, :], sm(slot)[:, 0, :], 1.0 / HD, None, ALU.mult))
                h.wait(v)
                if warm:
                    v.wait_ge(s_zz, i - 1)
                    v.wait_ge(s_sq, i - 1)
                v.tensor_tensor(heads(zb[:, slot, :, 0:P]), heads(xo.rearrange("p (k c) -> p k c", k=2)),
                                per_head(sm(slot)[:, 1, :]), ALU.subtract).then_inc(s_d, 1)

            def take(i, slot, warm):
                v.wait_ge(s_kvp, i + 1)
                if warm:
                    v.wait_ge(s_st[slot], i * 16 - 16 * slot)
                    v.wait_ge(s_r2, i - 1)
                v.tensor_tensor(kvs[:, slot, :], ps[:, 2 + slot, :], bkv, ALU.add).then_inc(s_kve, 1)
                v.scalar_tensor_tensor(qf[:, slot, :], ps[:, 4 + slot, 0:D], QSCALE, bqs, ALU.mult, ALU.add).then_inc(s_qe, 1)

            def scaled(i, slot):
                v.wait_ge(s_sq, i + 1)
                v.tensor_reduce(sm(slot)[:, 2, :], sq[:, slot, :].rearrange("p (h d) -> p h d", d=HD), X, ALU.add).then_inc(s_ss, 1)
                v.wait_ge(s_rt, i + 1)
                h.inc(v.tensor_scalar(sm(slot)[:, 3, :], sm(slot)[:, 3, :], LN_EPS, None, ALU.add))
                h.wait(v)
                h.inc(v.reciprocal(sm(slot)[:, 3, :], sm(slot)[:, 3, :]))
                h.wait(v)
                v.tensor_tensor(heads(zb[:, slot, :, 0:P]), heads(zb[:, slot, :, 0:P]),
                                per_head(sm(slot)[:, 3, :]), ALU.mult).then_inc(s_z, 1)

            def step(i, slot):
                h.at(i * 4)
                normal(i, slot)
                if not isinstance(i, int) or i >= 1:
                    take(i - 1, 1 - slot, not isinstance(i, int) or i >= 3)
                scaled(i, slot)
            v.wait_ge(s_c, NCONST)
            pairs(v, NB, step, 4)
            take(NB - 1, (NB - 1) % 2, True)

            m = Count(s_mix)
            v.wait_ge(s_zz, NB)
            m.inc(v.tensor_copy(zzs, zz_ps))
            m.wait(v)
            for k in range(2):
                m.inc(v.tensor_scalar(zsq[:, k, :], ones[:, :], zzs[:, k, P:P + 1], None, ALU.mult))
            v.wait_ge(s_mxp, 1)
            for k in range(2):
                vw, vb = vwb[:, k * P:k * P + P], vwb[:, D + k * P:D + k * P + P]
                if k:
                    v.wait_ge(s_bd, k)
                m.inc(v.tensor_scalar(mt[:, 0, :], vb, zzs[:, k, P:P + 1], None, ALU.mult))
                m.inc(v.tensor_tensor(mt[:, 1, :], zzs[:, k, 0:P], vw, ALU.mult))
                m.inc(v.tensor_tensor(mt[:, 2, :], ps[:, 0, k * P:k * P + P], vw, ALU.mult))
                m.wait(v)
                m.inc(v.tensor_tensor(mt[:, 0, :], mt[:, 0, :], mt[:, 1, :], ALU.add))
                m.inc(v.scalar_tensor_tensor(mt[:, 2, :], vb, float(N), mt[:, 2, :], ALU.mult, ALU.add))
                m.wait(v)
                m.inc(v.tensor_scalar(mt[:, 0, :], mt[:, 0, :], kwb[:, k:k + 1], 1.0 / N, ALU.mult, ALU.mult))
                m.inc(v.tensor_scalar(mt[:, 2, :], mt[:, 2, :], kwb[:, 2 + k:3 + k], 1.0 / N, ALU.mult, ALU.mult))
                m.wait(v)
                m.inc(v.tensor_tensor(mt[:, 0, :], mt[:, 0, :], mt[:, 2, :], ALU.add))
                m.wait(v)
                m.inc(v.tensor_tensor(mt[:, 0, :], mt[:, 0, :], hmask, ALU.mult))
                m.wait(v)
                v.tensor_tensor(bd[:, k, :], mt[:, 0, :], ident[:, :], ALU.add).then_inc(s_bd, 1)

        def act1(act):
            act.wait_ge(s_var, 1)
            act.activation(rs[:, 1, :], rs[:, 0, :], ACT.Sqrt).then_inc(s_std, 1)

            def parts(i, slot):
                act.wait_ge(s_qe, i + 1)
                act.activation(q_part(i, 0), qf[:, slot, :], ACT.Copy).then_inc(s_q1, 1)
                act.wait_ge(s_r1, i + 1)
                act.activation(q_part(i, 1), qr[:, slot, :], ACT.Copy).then_inc(s_q2, 1)

            def step(i, slot):
                warm = not isinstance(i, int) or i >= 2
                act.wait_ge(s_tr, i + 1)
                if warm:
                    act.wait_ge(s_st[slot], i * 16 - 16 * slot)
                    act.wait_ge(s_kvp, i - 1)
                act.activation(xnT[:, slot, :], ps[:, slot, 0:D], ACT.Copy).then_inc(s_xt, 1)
                act.wait_ge(s_d, i + 1)
                act.activation(sq[:, slot, :].rearrange("p (k c) -> p k c", k=2), zb[:, slot, :, 0:P],
                               ACT.Square).then_inc(s_sq, 1)
                act.wait_ge(s_ss, i + 1)
                act.activation(small[:, slot, 3 * H:4 * H], small[:, slot, 2 * H:3 * H], ACT.Sqrt,
                               scale=1.0 / (HD - 1)).then_inc(s_rt, 1)
                if not isinstance(i, int) or i >= 1:
                    parts(i - 1, 1 - slot)
            pairs(act, NB, step)
            parts(NB - 1, (NB - 1) % 2)

        def pe1(pe):
            pe.wait_ge(s_c, NCONST)
            pe.matmul(ps[:, 6, :], zero16[0:1, 0:P], zero16[0:1, :], start=True, stop=False, skip_group_check=True)

            def z_products(i, slot):
                pe.wait_ge(s_z, i + 1)
                for k in range(2):
                    last = pe.matmul(zz_ps[:, k, :], zb[:, slot, k, 0:P], zb[:, slot, k, :], start=False,
                                     stop=True, skip_group_check=True)
                last.then_inc(s_zz, 1)

            def step(i, slot):
                warm = not isinstance(i, int) or i >= 2
                pe.wait_ge(s_xn, i + 1)
                if warm:
                    pe.wait_ge(s_xt, i - 1)
                for k in range(2):
                    last = pe.transpose(ps[:, slot, k * P:k * P + P], xn[:, slot, k * P:k * P + P], ident[:, :])
                last.then_inc(s_tr, 1)
                if not isinstance(i, int) or i >= 1:
                    z_products(i - 1, 1 - slot)
                pe.wait_ge(s_xt, i + 1)
                if warm:
                    pe.wait_ge(s_kve, i - 1)
                    pe.wait_ge(s_qe, i - 1)
                for w, o in ((wkv, ps[:, 2 + slot, :]), (wq, ps[:, 4 + slot, 0:D])):
                    for k in range(2):
                        last = pe.matmul(o, xnT[:, slot, k * P:k * P + P], w[:, k, :], start=(k == 0), stop=(k == 1))
                last.then_inc(s_kvp, 1)
            pairs(pe, NB, step)
            z_products(NB - 1, (NB - 1) % 2)
            pe.wait_ge(s_mix, 3)
            for k in range(2):
                last = pe.matmul(ps[:, 0, k * P:k * P + P], zsq[:, k, :], ident[:, :], start=True, stop=True)
            last.then_inc(s_mxp, 1)

        def span(eng, c, earlier=0):
            row = tab[0:1, bass.ds(c, 1), :].rearrange("p a d -> p (a d)")
            first = isinstance(c, int) and c == 0
            return (eng.value_load(row[:, 0:1], min_val=0, max_val=NB - 1),
                    eng.value_load(row[:, 1:2], min_val=1, max_val=NB),
                    0 if first else eng.value_load(row[:, 2:3], min_val=earlier, max_val=NC * NB))

        def others(eng, at, body):
            b0, n, v0 = at
            with eng.If(n > 1):
                with eng.Fori(1, n) as j:
                    body(nc.s_assert_within(b0 + j, 1, NB - 1), v0 + j)

        def groups(unit, group_end, eng):
            for k in range(GC):
                unit(0, k, 0, False, True)
            group_end(0, 0, False)
            with eng.Fori(0, (NG - 2) // 2) as t:
                for u in range(2):
                    g, par = t * 2 + (1 + u), (1 + u) % 2
                    for k in range(GC):
                        unit(g, k, par, True, True)
                    group_end(g, par, False)
            for k in range(GC):
                unit(NG - 1, k, (NG - 1) % 2, True, k < GC - 1)
            group_end(NG - 1, (NG - 1) % 2, True)

        def following(g, k, par):
            return (g, k + 1, par) if k < GC - 1 else (g + 1, 0, 1 - par)

        def sync2(sp):
            def load(g, par):
                if not isinstance(g, int) or g >= 2:
                    sp.wait_ge(s_grp, g - 1)
                for t, name in ((src, "src"), (dst, "dst"), (ew, "ew")):
                    sp.dma_start(t[:, par, :], a[name][bass.ds(g * P, P), :]).then_inc(s_in[par], 16)
            pairs(sp, NG, load)

        def edges_in(eng, g, par):
            eng.wait_ge(s_in[par], g * 24 + (48 - 24 * par))

        def pool2(pool):
            for slot, n in ((0, (NB + 1) // 2), (1, NB // 2)):
                pool.wait_ge(s_st[slot], 32 * n)
            pool.wait_ge(s_bd, 2)
            pool.wait_ge(s_r2, NB)
            pool.wait_ge(s_xz, 16)
            pool.nop(nofuse=True)

            def gather(g, par):
                edges_in(pool, g, par)
                pool.nop(nofuse=True)
                for k in range(GC):
                    if not isinstance(g, int) or g >= 2:
                        pool.wait_ge(s_pq, g * GC + (k - 2))
                        pool.nop(nofuse=True)
                    for t in range(TC):
                        pool.indirect_dma_start(
                            out=ring[:, par * GC + k, t, :], out_offset=None, in_=kv_d,
                            in_offset=bass.IndirectOffsetOnAxis(ap=src[:, par, k * TC + t:k * TC + t + 1], axis=0),
                        ).then_inc(s_g[par * GC + k], 16)
            pairs(pool, NG, gather)

        def dve2(v):
            la, lb, lp, lm, lz = Count(s_la), Count(s_lb), Count(s_lp), Count(s_lm), Count(s_zl)

            def onehots(out_t, place, done):
                for j in range(TC):
                    last = v.tensor_scalar(out_t[:, j, :], iota16[:, :], place[:, j:j + 1], None, ALU.is_equal)
                last.then_inc(done, 1)

            def spread_one(b, vis, x, par, k, cold=False):
                if not cold:
                    v.wait_ge(s_T, vis)
                la.at(vis)
                la.inc(v.tensor_scalar(locA[:, x, :], dst[:, par, k * TC:k * TC + TC], blk0[:, bass.ds(b, 1)], None,
                                       ALU.subtract))
                la.wait(v)
                onehots(S16[:, :, :], locA[:, x, :], s_S16)

            def sum_one(b, vis, x, k, par):
                lb.at(vis * 2)
                v.tensor_tensor(fd[:, :], blk(Mblk, b), Mn[:, par, H:H + 2], ALU.subtract).then_inc(s_fd, 1)
                v.wait_ge(s_fd, vis + 1)
                lb.inc(v.tensor_scalar(locB[:, x, :], dstB[:, k * TC:k * TC + TC], blk0[:, bass.ds(b, 1)], None,
                                       ALU.subtract))
                lb.inc(v.tensor_copy(blk(Mblk, b), Mn[:, par, H:H + 2]))
                lb.wait(v)
                onehots(S32[:, :, :], locB[:, x, :], s_S32)

            def add_one(b, vis, x):
                v.wait_ge(s_O, vis + 1)
                v.wait_ge(s_f, vis + 1)
                for k in range(2):
                    t = acc[:, bass.ds(b, 1), k, :].rearrange("p a n -> p (a n)")
                    last = v.scalar_tensor_tensor(t, t, fe[:, k:k + 1], ps[:, 6, k * P:k * P + P],
                                                  ALU.mult, ALU.add)
                last.then_inc(s_acc, 1)

            def scores(g, k, par):
                _, n, v0 = span(v, g * GC + k)
                v.wait_ge(s_Q, v0 + n)
                slot = par * GC + k
                v.wait_ge(s_g[slot], g * 32 + (64 - 32 * par))
                kr = ring[:, slot, :, 0:D]
                bank = 2 * (k % 2)
                v.tensor_copy(nvs[:, k * TC:k * TC + TC, :],
                              ps[:, 5 + 2 * (k % 2), 0:3 * TC].rearrange("p (t j) -> p t j", j=3))
                lp.at(g * GC + k)
                lp.inc(v.tensor_tensor(kr, kr, ps[:, bank:bank + 2, :].rearrange("p a (t d) -> p (a t) d", d=D), ALU.mult))
                lp.wait(v)
                v.tensor_reduce(sc[:, k * TC:k * TC + TC, :], kr.rearrange("p t (h d) -> p t h d", d=HD), X,
                                ALU.add).then_inc(s_pq, 1)

            def sum_exps(g, par):
                v.wait_ge(s_fz, g + 1)
                lz.at(g * 3)
                lz.inc(v.tensor_reduce(zsum[:, :], prob[:, :, :].rearrange("p t h -> p h t"), X, ALU.add))
                lz.inc(v.tensor_tensor(Zp[:, par, :], Zp[:, 1 - par, :], fz[:, par, :], ALU.mult))
                lz.wait(v)
                lz.inc(v.tensor_tensor(Zp[:, par, :], Zp[:, par, :], zsum[:, :], ALU.add))

            def sum_first(g, k, par):
                if k == 0:
                    v.wait_ge(s_pe, g + 1)
                    v.wait_ge(s_grp, g + 1)
                w = ring[:, par * GC + k, :, D:2 * D].rearrange("p t (h d) -> p t h d", d=HD)
                pr = prob[:, k * TC:k * TC + TC, :].unsqueeze(3).to_broadcast([P, TC, H, HD])
                v.tensor_tensor(w, w, pr, ALU.mult).then_inc(s_msg, 1)
                if k == 0:
                    sum_exps(g, par)
                at = span(v, g * GC + k)
                sum_one(at[0], at[2], 0, k, par)
                return at

            def sum_rest(at, k, par):
                add_one(at[0], at[2], 0)

                def more(b, vis):
                    sum_one(b, vis, 1, k, par)
                    add_one(b, vis, 1)
                others(v, at, more)

            def unit(g, k, par, old, new):
                if new:
                    ng, nk, npar = following(g, k, par)
                    if nk == 0:
                        edges_in(v, ng, npar)
                    nat = span(v, ng * GC + nk, 1)
                    spread_one(nat[0], nat[2], 0, npar, nk)
                if old:
                    oat = sum_first(g - 1, k, 1 - par)
                if new:
                    others(v, nat, lambda b, vis: spread_one(b, vis, 1, npar, nk))
                scores(g, k, par)
                if old:
                    sum_rest(oat, k, 1 - par)

            def group_end(g, par, last):
                lm.at(g * KM)

                def per_head(row):
                    return row.unsqueeze(1).to_broadcast([P, GT, H])

                def per_edge(col):
                    return col.unsqueeze(2).to_broadcast([P, GT, H])
                v.wait_ge(s_pq, g * GC + GC)
                lm.inc(v.tensor_tensor(tf[:, 0, :], nvs[:, :, 0], nvs[:, :, 1], ALU.add))
                lm.wait(v)
                lm.inc(v.tensor_tensor(tf[:, 1, :], tf[:, 0, :], nvs[:, :, 2], ALU.add))
                lm.wait(v)
                lm.inc(v.tensor_tensor(tf[:, 2, :], ew[:, par, :], tf[:, 1, :], ALU.subtract))
                lm.wait(v)
                v.scalar_tensor_tensor(tf[:, 3, :], tf[:, 2, :], -1.0, tf[:, 2, :], ALU.mult, ALU.max).then_inc(s_abs, 1)
                lm.inc(v.tensor_scalar(tf[:, 0, :], tf[:, 2, :], 0.0, None, ALU.is_gt))
                lm.wait(v)
                lm.inc(v.scalar_tensor_tensor(tf[:, 1, :], tf[:, 2, :], 0.0, tf[:, 0, :], ALU.is_lt, ALU.subtract))
                lm.wait(v)
                lm.inc(v.tensor_tensor(tw[:, 0, :, :], per_edge(tf[:, 1, :]), per_head(wtb[:, 0, :]), ALU.mult))
                lm.wait(v)
                lm.inc(v.tensor_tensor(tw[:, 0, :, :], tw[:, 0, :, :], per_head(wtb[:, 2, :]), ALU.add))
                v.wait_ge(s_ln, g + 1)
                lm.inc(v.tensor_tensor(tw[:, 1, :, :], per_edge(tf[:, 4, :]), per_head(wtb[:, 1, :]), ALU.mult))
                lm.wait(v)
                lm.inc(v.tensor_tensor(tw[:, 0, :, :], tw[:, 0, :, :], tw[:, 1, :, :], ALU.add))
                lm.wait(v)
                lm.inc(v.tensor_tensor(sc[:, :, :], sc[:, :, :], tw[:, 0, :, :], ALU.add))
                lm.wait(v)
                if last:
                    lm.inc(v.tensor_scalar(tf[:, 5, :], dst[:, par, :], float(N), NEG, ALU.is_ge, ALU.mult))
                    lm.wait(v)
                    lm.inc(v.tensor_tensor(sc[:, :, :], sc[:, :, :], per_edge(tf[:, 5, :]), ALU.add))
                    lm.wait(v)
                lm.inc(v.tensor_reduce(mxp[:, :], sc[:, :, :].rearrange("p t h -> p h t"), X, ALU.max))
                lm.wait(v)
                v.tensor_tensor(mxp[:, :], mxp[:, :], Mn[:, 1 - par, 0:H], ALU.max).then_inc(s_mx, 1)
                v.wait_ge(s_mt, g + 1)
                lm.inc(v.tensor_reduce(m8[:, :], ps[0:H, 6, D:D + P], X, ALU.max))
                lm.wait(v)
                v.tensor_scalar(dg[:, :], ident[0:H, 0:H], m8[:, 0:1], None, ALU.mult).then_inc(s_m8, 1)
                v.wait_ge(s_mb, g + 1)
                lm.inc(v.tensor_copy(Mn[:, par, :], ps[:, 6, D + P:D + P + H + 2]))
                lm.wait(v)
                lm.inc(v.tensor_tensor(sc[:, :, :], sc[:, :, :], per_head(Mn[:, par, 0:H]), ALU.subtract))
                v.tensor_copy(dstB[:, :], dst[:, par, :]).then_inc(s_grp, 1)
                v.tensor_tensor(fz[:, par, :], Mn[:, 1 - par, 0:H], Mn[:, par, 0:H], ALU.subtract).then_inc(s_sh, 1)
                assert last or lm.n == KM
            KM = 14

            v.memset(Mn[:, 1, :], NEG).then_inc(s_grp0, 1)
            v.memset(Zp[:, 1, :], 0.0).then_inc(s_grp0, 1)
            v.memset(z8[:, :], 0.0).then_inc(s_acc, 1)
            v.wait_ge(s_grp0, 2)
            v.wait_ge(s_tab, 4)
            v.wait_ge(s_az, NB)
            edges_in(v, 0, 0)
            at = span(v, 0)
            spread_one(at[0], 0, 0, 0, 0, cold=True)
            others(v, at, lambda b, vis: spread_one(b, vis, 1, 0, 0))
            groups(unit, group_end, v)
            for k in range(GC):
                par = (NG - 1) % 2
                sum_rest(sum_first(NG - 1, k, par), k, par)

            f = Count(s_fin)
            par = (NG - 1) % 2
            f.inc(v.tensor_tensor(G[:, :, :], Mblk[:, :, :], Mn[:, par, H:H + 2].unsqueeze(1).to_broadcast([P, NB, 2]),
                                  ALU.subtract))
            v.wait_ge(s_fp, 1)
            f.inc(v.reciprocal(z8[:, 0:1], ps[0:H, 5, 0:1]))
            v.wait_ge(s_fp, 2)
            f.inc(v.tensor_copy(Mn[:, 1 - par, 0:2], ps[:, 5, 2:4]))
            f.wait(v)
            v.wait_ge(s_fa, 1)
            v.tensor_tensor(G[:, :, :], G[:, :, :], Mn[:, 1 - par, 0:2].unsqueeze(1).to_broadcast([P, NB, 2]),
                            ALU.mult).then_inc(s_G, 1)

        def act2(act):
            def turn(vis, x, cold=False):
                act.wait_ge(s_T, vis + 1)
                if not cold:
                    act.wait_ge(s_Q, vis)
                act.activation(ST[:, :, :].rearrange("p t r -> p (t r)"),
                               turned[:, x * CH:x * CH + CH], ACT.Copy).then_inc(s_ST, 1)

            def rescale(vis):
                act.wait_ge(s_fd, vis + 1)
                act.activation(fe[:, :], fd[:, :], ACT.Exp).then_inc(s_f, 1)

            def unit(g, k, par, old, new):
                if new:
                    nat = span(act, g * GC + (k + 1), 1)
                    turn(nat[2], 0)
                if old:
                    oat = span(act, g * GC + (k - GC))
                    rescale(oat[2])
                if new:
                    others(act, nat, lambda b, vis: turn(vis, 1))
                if old:
                    others(act, oat, lambda b, vis: rescale(vis))

            def group_end(g, par, last):
                act.wait_ge(s_abs, g + 1)
                act.activation(tf[:, 4, :], tf[:, 3, :], ACT.Ln, bias=1.0, scale=1.0 / 3600.0).then_inc(s_ln, 1)
                act.wait_ge(s_sh, g + 1)
                act.activation(prob[:, :, :], sc[:, :, :], ACT.Exp).then_inc(s_pe, 1)
                act.activation(fz[:, par, :], fz[:, par, :], ACT.Exp).then_inc(s_fz, 1)
            act.wait_ge(s_tab, 4)
            at = span(act, 0)
            turn(0, 0, cold=True)
            others(act, at, lambda b, vis: turn(vis, 1))
            groups(unit, group_end, act)
            for k in range(GC):
                oat = span(act, (NG - 1) * GC + k)
                rescale(oat[2])
                others(act, oat, lambda b, vis: rescale(vis))
            act.wait_ge(s_fin, 1)
            act.activation(G[:, :, :], G[:, :, :], ACT.Exp).then_inc(s_fa, 1)

        turned = ps[:, 4, :].bitcast(BF16)

        def pe2(pe):
            def turn(vis, x, cold=False):
                pe.wait_ge(s_S16, vis + 1)
                if not cold:
                    pe.wait_ge(s_ST, vis)
                for t in range(TC):
                    last = pe.transpose(turned[:, x * CH + t * P:x * CH + t * P + P], S16[:, t, :], ident16[:, :])
                last.then_inc(s_T, 1)

            def spread(b, vis, x, k, par, first):
                pe.wait_ge(s_ST, vis + 1)
                bank = 2 * (k % 2)
                for t in range(TC):
                    w = ST[:, t, :]
                    o = ps[:, bank + t // 2, (t % 2) * D:(t % 2) * D + D]
                    for j in range(3):
                        pe.matmul(o, w, q_part(b, j), start=first and t % 2 == 0 and j == 0, stop=True,
                                  skip_group_check=True)
                    last = pe.matmul(ps[:, 5 + 2 * (k % 2), 3 * t:3 * t + 3], w, flat(nv3[:, bass.ds(b, 1), 0:3]),
                                     start=first and t == 0, stop=True, skip_group_check=True)
                last.then_inc(s_Q, 1)

            def sums(vis, x, k, par):
                pe.wait_ge(s_S32, vis + 1)
                pe.wait_ge(s_acc, vis + 1)
                slot = par * GC + k
                for h in range(2):
                    for t in range(TC):
                        last = pe.matmul(ps[:, 6, h * P:h * P + P], ring[:, slot, t, D + h * P:D + h * P + P],
                                         S32[:, t, :], start=(h == 0 and t == 0), stop=True, skip_group_check=True)
                last.then_inc(s_O, 1)

            def sums_first(g, k, par):
                at = span(pe, g * GC + k)
                pe.wait_ge(s_msg, g * GC + (k + 1))
                sums(at[2], 0, k, par)
                return at

            def sums_rest(at, k, par):
                others(pe, at, lambda b, vis: sums(vis, 1, k, par))

            def unit(g, k, par, old, new):
                if new:
                    ng, nk, npar = following(g, k, par)
                    nat = span(pe, ng * GC + nk, 1)
                    turn(nat[2], 0)
                if old:
                    oat = sums_first(g - 1, k, 1 - par)
                if new:
                    if not isinstance(g, int) or g > 0 or k > 0:
                        pe.wait_ge(s_pq, g * GC + k)
                    spread(nat[0], nat[2], 0, nk, npar, True)

                    def more(b, vis):
                        turn(vis, 1)
                        spread(b, vis, 1, nk, npar, False)
                    others(pe, nat, more)
                if old:
                    sums_rest(oat, k, 1 - par)

            def group_end(g, par, last):
                pe.wait_ge(s_mx, g + 1)
                pe.transpose(ps[0:H, 6, D:D + P], mxp[:, :], ident[:, :]).then_inc(s_mt, 1)
                pe.wait_ge(s_m8, g + 1)
                pe.matmul(ps[:, 6, D + P:D + P + H], ones[0:H, :], dg[:, :], start=True, stop=True, skip_group_check=True)
                for k in range(2):
                    last_mm = pe.matmul(ps[:, 6, D + P + H + k:D + P + H + k + 1], headind[:, k, :], m8[:, :],
                                        start=True, stop=True, skip_group_check=True)
                last_mm.then_inc(s_mb, 1)
            pe.wait_ge(s_bd, 2)
            pe.wait_ge(s_tab, 4)
            at = span(pe, 0)
            turn(0, 0, cold=True)
            spread(at[0], 0, 0, 0, 0, True)

            def more(b, vis):
                turn(vis, 1)
                spread(b, vis, 1, 0, 0, False)
            others(pe, at, more)
            groups(unit, group_end, pe)
            par = (NG - 1) % 2
            for k in range(GC):
                sums_rest(sums_first(NG - 1, k, par), k, par)
            pe.wait_ge(s_zl, 3 * NG)
            pe.matmul(ps[0:H, 5, 0:1], Zp[:, par, :], ones[:, 0:1], start=True, stop=True, skip_group_check=True).then_inc(s_fp, 1)
            pe.wait_ge(s_fin, 2)
            for k in range(2):
                last = pe.matmul(ps[:, 5, 2 + k:3 + k], headind[:, k, :], z8[:, 0:1], start=True, stop=True, skip_group_check=True)
            last.then_inc(s_fp, 1)

        EW = 2 * F
        w2 = R2[:, 0:NX * EW].rearrange("p (e c d) -> p e c d", e=NX, c=FC)
        w1 = R2[:, NX * EW:(NX + 2) * EW].rearrange("p (s k f) -> p s k f", s=2, k=2)
        tops = [(NX + 2) * EW]

        def top(n, m):
            v = R2[:, tops[0]:tops[0] + n * m].rearrange("p (a b) -> p a b", b=m)
            tops[0] += n * m
            assert tops[0] <= QW + KVW
            return v
        as3, xt3, x3, wo = top(2, D), top(2, D), top(2, D), top(2, D)
        bob = top(1, D)[:, 0, :]

        def gate_work(n=NB * NX):
            return top(1, n)[:, 0, :]

        def tok(v):
            return v.rearrange("p (i e) -> p i e", e=NX)
        gs, rank, oh1, oh2, comb, gt, excl, cum = (tok(gate_work()) for _ in range(8))
        wg = gate_work(2 * NX).rearrange("p (k e) -> p k e", k=2)
        bg = gate_work(NX)
        upper = gate_work(P)
        tl = gate_work(6 * NX).rearrange("p (a e) -> p a e", a=6)
        tli = gate_work(NX).bitcast(I32)
        ms = gate_work(3 * NB).rearrange("p (a i) -> p a i", a=3)
        etf = gate_work(2 * P)[0:1, :].rearrange("p (a j) -> p a j", a=2)
        b2 = gate_work(D)[0:NX, :]
        cs = top(2, NX)
        bnst3 = S32[:, :, :].rearrange("p t r -> p (t r)")[:, 0:NB * 6].rearrange("p (i s) -> p i s", s=6)
        fw = [0]

        def ffn_work(*shape):
            n = 1
            for s in shape:
                n *= s
            v = R1[:, fw[0]:fw[0] + n]
            fw[0] += n
            if len(shape) == 2:
                return v.rearrange("p (a b) -> p a b", b=shape[1])
            return v.rearrange("p (a b c) -> p a b c", b=shape[1], c=shape[2])
        xs, xsT, ys = ffn_work(2, D), ffn_work(2, D), ffn_work(2, D)
        hT = ffn_work(2, FC, P)
        y1, y2, x5, o5 = ffn_work(2, D), ffn_work(2, D), ffn_work(2, D), ffn_work(2, D)

        def both(slot, i):
            return i * 8 + (16 - 8 * slot)

        def late(i, n=2):
            return not isinstance(i, int) or i >= n

        def stage3_sync(sp):
            sp.wait_ge(s_G, 1)
            sp.dma_start(wo, a["wo"].rearrange("(k p) n -> p k n", p=P)).then_inc(s_w3, 16)
            sp.dma_start(bob, a["bo"].partition_broadcast(P)).then_inc(s_w3, 16)
            sp.dma_start(wg, a["wg"].rearrange("(k p) n -> p k n", p=P)).then_inc(s_w3, 16)
            sp.dma_start(bg, a["bg"].partition_broadcast(P)).then_inc(s_w3, 16)
            sp.dma_start(upper, a["upper"]).then_inc(s_w3, 16)
            sp.dma_start(b1[:, :, :], a["b1"].rearrange("e (c p) -> p e c", p=P), allow_slow_non_contiguous=True).then_inc(s_w3, 16)
            sp.dma_start(b2, a["b2"]).then_inc(s_w3, 16)

            def step(i, slot):
                if late(i):
                    sp.wait_ge(s_p3, i - 1)
                    sp.wait_ge(s_x2, i - 1)
                sp.dma_start(xt3[:, slot, :], xnT_d[bass.ds(i * P, P), :]).then_inc(s_in3[slot], 16)
                sp.dma_start(x3[:, slot, :], a["x"][bass.ds(i * P, P), :]).then_inc(s_in3[slot], 16)
            pairs(sp, NB, step)
            sp.dma_start(w2, a["w2"].rearrange("e (c p) d -> p e c d", p=P)).then_inc(s_we, 16)

            def store(i, slot):
                sp.wait_ge(s_x2b, i + 1)
                sp.dma_start(x2_d[bass.ds(i * P, P), :], as3[:, slot, :]).then_inc(s_x2s[slot], 16)
            pairs(sp, NB, store, 0)

        def stage3_pool(pool):
            pool.wait_ge(s_w3, 7 * 16)

            def step(i, slot):
                pool.wait_ge(s_in3[slot], i * 16 + (32 - 16 * slot))
                pool.tensor_tensor(x3[:, slot, :], x3[:, slot, :], bob, ALU.add).then_inc(s_xb, 1)
            pairs(pool, NB, step, 0)

            def scatter(i, slot):
                pool.wait_ge(s_posx, i + 1)
                if late(i):
                    pool.wait_ge(s_sc[slot], both(slot, i - 2) * 2)
                pool.tensor_copy(place[:, slot, :], blk(pos, i)).then_inc(s_pl, 1)
                pool.wait_ge(s_pl, i + 1)
                pool.nop(nofuse=True)
                for j in range(2):
                    pool.indirect_dma_start(
                        out=xs_d, out_offset=bass.IndirectOffsetOnAxis(ap=place[:, slot, j:j + 1], axis=0),
                        in_=x3[:, slot, :], in_offset=None).then_inc(s_sc[slot], 16)
            pairs(pool, NB, scatter)

            pool.wait_ge(s_yst[0], 16 * ((NT + 1) // 2))
            pool.wait_ge(s_yst[1], 16 * (NT // 2))

            def collect(i, slot):
                if late(i):
                    pool.wait_ge(s_o, i - 1)
                pool.tensor_copy(place[:, slot, :], blk(pos, i)).then_inc(s_pl, 1)
                pool.wait_ge(s_pl, i + (NB + 1))
                pool.nop(nofuse=True)
                for j, y in enumerate((y1, y2)):
                    pool.indirect_dma_start(
                        out=y[:, slot, :], out_offset=None, in_=ys_d,
                        in_offset=bass.IndirectOffsetOnAxis(ap=place[:, slot, j:j + 1], axis=0)).then_inc(s_yg[slot], 16)
            pairs(pool, NB, collect)

        def stage3_act(act):
            act.wait_ge(s_G, 1)

            def step(i, slot):
                if late(i):
                    act.wait_ge(s_p3, i - 1)
                for k in range(2):
                    last = act.activation(as3[:, slot, k * P:k * P + P],
                                          acc[:, bass.ds(i, 1), k, :].rearrange("p a n -> p (a n)"), ACT.Copy,
                                          scale=flat(G[:, bass.ds(i, 1), k:k + 1]))
                last.then_inc(s_as, 1)
            pairs(act, NB, step)
            act.wait_ge(s_var, 2)
            act.activation(rs[:, 1, :], rs[:, 0, :], ACT.Sqrt).then_inc(s_std, 1)

            def gate(i, slot):
                act.wait_ge(s_ft, i + 1)
                if late(i):
                    act.wait_ge(s_gp, i - 1)
                act.activation(xt3[:, slot, :], ps[:, 2 + slot, 0:D], ACT.Copy).then_inc(s_fc, 1)
            pairs(act, NB, gate)
            act.wait_ge(s_dm, 1)
            act.activation(ms[:, 1, :], ms[:, 0, :], ACT.Exp).then_inc(s_em, 1)

            def bias(i, slot):
                act.wait_ge(s_ct, i + 1)
                if late(i):
                    act.wait_ge(s_bp, i - 1)
                act.activation(cT[:, slot, :], ps[0:NX, slot, 0:P], ACT.Copy).then_inc(s_cc, 1)
            pairs(act, NB, bias)

            def hidden(j, slot):
                e = act.value_load(etab[0:1, bass.ds(j, 1)], min_val=0, max_val=NX - 1)
                act.wait_ge(s_h1[0], j + 1)
                if late(j):
                    act.wait_ge(s_y, j - 1)
                for c in range(FC // 2):
                    last = act.activation(hT[:, slot, c, :], ps[:, 2 + 2 * slot, c * P:c * P + P], ACT.Relu,
                                          bias=flat(b1[:, bass.ds(e, 1), c:c + 1]))
                last.then_inc(s_ha, 1)
            pairs(act, NT, hidden)

        def stage3_pe(pe):
            pe.wait_ge(s_w3, 7 * 16)

            def step(i, slot):
                pe.wait_ge(s_as, i + 1)
                pe.wait_ge(s_in3[slot], i * 16 + (32 - 16 * slot))
                if late(i):
                    pe.wait_ge(s_x2, i - 1)
                o = ps[:, slot, 0:D]
                for k in range(2):
                    pe.matmul(o, as3[:, slot, k * P:k * P + P], wo[:, k, :], start=(k == 0), stop=False, skip_group_check=True)
                for k in range(2):
                    last = pe.matmul(o[:, k * P:k * P + P], xt3[:, slot, k * P:k * P + P], bd[:, k, :],
                                     start=False, stop=True, skip_group_check=True)
                last.then_inc(s_p3, 1)
            pairs(pe, NB, step)

            def gate(i, slot):
                pe.wait_ge(s_xf, i + 1)
                if late(i):
                    pe.wait_ge(s_fc, i - 1)
                for k in range(2):
                    last = pe.transpose(ps[:, 2 + slot, k * P:k * P + P], x3[:, slot, k * P:k * P + P], ident[:, :])
                last.then_inc(s_ft, 1)
                pe.wait_ge(s_fc, i + 1)
                if late(i):
                    pe.wait_ge(s_g2, i - 1)
                for k in range(2):
                    last = pe.matmul(ps[:, 4 + slot, 0:NX], xt3[:, slot, k * P:k * P + P], wg[:, k, :],
                                     start=(k == 0), stop=(k == 1))
                last.then_inc(s_gp, 1)
            pairs(pe, NB, gate)
            pe.wait_ge(s_oh, 1)
            chosen = gt.rearrange("p i e -> p (i e)")
            pe.matmul(ps[:, 6, 0:NB * NX], upper, chosen, start=True, stop=True)
            pe.matmul(ps[:, 7, 0:NB * NX], ones[:, :], chosen, start=True, stop=True).then_inc(s_cnt, 1)

            def bias(i, slot):
                pe.wait_ge(s_cs, i + 1)
                if late(i):
                    pe.wait_ge(s_cc, i - 1)
                pe.transpose(ps[0:NX, slot, 0:P], cs[:, slot, :], ident[:, :]).then_inc(s_ct, 1)
                pe.wait_ge(s_cc, i + 1)
                if late(i):
                    pe.wait_ge(s_x2b, i - 1)
                pe.matmul(ps[:, 2 + slot, 0:D], cT[:, slot, :], b2, start=True, stop=True).then_inc(s_bp, 1)
            pairs(pe, NB, bias)

            def turn(j, slot):
                pe.wait_ge(s_xs[slot], both(slot, j))
                if late(j):
                    pe.wait_ge(s_xc, j - 1)
                for k in range(2):
                    last = pe.transpose(ps[:, slot, k * P:k * P + P], xs[:, slot, k * P:k * P + P], ident[:, :])
                last.then_inc(s_xt4, 1)

            def first_layer(j, slot):
                pe.wait_ge(s_xc, j + 1)
                pe.wait_ge(s_w1[slot], both(slot, j))
                for half, taken in ((0, s_ha), (1, s_hd)):
                    if late(j):
                        pe.wait_ge(taken, j - 1)
                    for c in range(FC // 2):
                        f = half * (F // 2) + c * P
                        for k in range(2):
                            last = pe.matmul(ps[:, 2 + 2 * slot + half, c * P:c * P + P], w1[:, slot, k, f:f + P],
                                             xsT[:, slot, k * P:k * P + P], start=(k == 0), stop=(k == 1))
                    last.then_inc(s_h1[half], 1)

            def second_layer(j, slot):
                e = pe.value_load(etab[0:1, bass.ds(j, 1)], min_val=0, max_val=NX - 1)
                pe.wait_ge(s_ha, j + 1)
                pe.wait_ge(s_hd, j + 1)
                if late(j):
                    pe.wait_ge(s_yc, j - 1)
                for c in range(FC):
                    last = pe.matmul(ps[:, 6 + slot, 0:D], hT[:, slot, c, :],
                                     w2[:, bass.ds(e, 1), c, :].rearrange("p a d -> p (a d)"),
                                     start=(c == 0), stop=(c == FC - 1))
                last.then_inc(s_y, 1)
            pe.wait_ge(s_etab, 1)
            pe.wait_ge(s_we, 16)
            pe.wait_ge(s_x2b, NB)
            turn(0, 0)

            def work4(j, slot):
                if not isinstance(j, int) or j < NT - 1:
                    turn(j + 1, 1 - slot)
                first_layer(j, slot)
                if late(j, 1):
                    second_layer(j - 1, 1 - slot)
            ffn_steps(pe, work4)
            second_layer(NT - 1, (NT - 1) % 2)

        def ffn_steps(eng, body):
            body(0, 0)
            body(1, 1)
            body(2, 0)
            body(3, 1)
            turns = (NT - 6) // 2
            with eng.Fori(0, turns) as t:
                body(t * 2 + 4, 0)
                body(t * 2 + 5, 1)
            for j in range(4 + 2 * turns, NT):
                body(j, j % 2)

        def stage3_dve(v):
            def step(i, slot):
                v.wait_ge(s_p3, i + 1)
                v.wait_ge(s_xb, i + 1)
                v.tensor_tensor(blk(x_sb, i), ps[:, slot, 0:D], x3[:, slot, :], ALU.add).then_inc(s_x2, 1)
                v.wait_ge(s_x2, i + 1)
                v.bn_stats(blk(bnst3, i), blk(x_sb, i)).then_inc(s_bn, 1)
            pairs(v, NB, step, 0)
            c = Count(s_v3)
            v.wait_ge(s_bn, NB)
            for i in range(NB):
                c.inc(v.bn_aggr(mv[:, i, :], bnst3[:, i, :]))
            c.wait(v)
            v.tensor_scalar(rs[:, 0, :], mv[:, :, 1], LN_EPS, None, ALU.add).then_inc(s_var, 1)
            v.wait_ge(s_std, 2)
            rstd(v, c)

            def normal(i, slot, done):
                v.tensor_scalar(x3[:, slot, :], blk(x_sb, i), flat(mv[:, bass.ds(i, 1), 0:1]), rs[:, 2, bass.ds(i, 1)],
                                ALU.subtract, ALU.mult).then_inc(done, 1)

            def take_gate(i, slot):
                v.wait_ge(s_gp, i + 1)
                v.tensor_tensor(blk(gs, i), ps[:, 4 + slot, 0:NX], bg, ALU.add).then_inc(s_g2, 1)

            def gate(i, slot):
                if late(i):
                    v.wait_ge(s_ft, i - 1)
                normal(i, slot, s_xf)
                if late(i, 1):
                    take_gate(i - 1, 1 - slot)
            pairs(v, NB, gate)
            take_gate(NB - 1, (NB - 1) % 2)
            v.wait_ge(s_g2, NB)
            c.inc(v.memset(rank, 0.0))
            for j in range(NX):
                c.wait(v)
                g = gs[:, :, j:j + 1]
                c.inc(v.tensor_tensor(gt[:, :, 0:j + 1], g.to_broadcast([P, NB, j + 1]), gs[:, :, 0:j + 1], ALU.is_gt))
                if j < NX - 1:
                    c.inc(v.tensor_tensor(gt[:, :, j + 1:NX], g.to_broadcast([P, NB, NX - 1 - j]), gs[:, :, j + 1:NX], ALU.is_ge))
                c.wait(v)
                c.inc(v.tensor_tensor(rank, rank, gt, ALU.add))
            c.wait(v)
            c.inc(v.tensor_scalar(oh1, rank, 0.0, None, ALU.is_equal))
            c.inc(v.tensor_scalar(oh2, rank, 1.0, None, ALU.is_equal))
            c.wait(v)
            v.tensor_tensor(gt, oh1, oh2, ALU.add).then_inc(s_oh, 1)
            c.inc(v.tensor_tensor(comb, gs, oh1, ALU.mult))
            c.inc(v.tensor_tensor(cum, gs, oh2, ALU.mult))
            c.wait(v)
            c.inc(v.tensor_reduce(ms[:, 0, :], comb, X, ALU.add))
            c.inc(v.tensor_reduce(ms[:, 1, :], cum, X, ALU.add))
            c.wait(v)
            v.tensor_tensor(ms[:, 0, :], ms[:, 1, :], ms[:, 0, :], ALU.subtract).then_inc(s_dm, 1)
            v.wait_ge(s_em, 1)
            c.inc(v.tensor_scalar(ms[:, 2, :], ms[:, 1, :], 1.0, None, ALU.add))
            c.wait(v)
            c.inc(v.reciprocal(pw[:, 0, :], ms[:, 2, :]))
            c.wait(v)
            c.inc(v.tensor_tensor(pw[:, 1, :], ms[:, 1, :], pw[:, 0, :], ALU.mult))
            c.wait(v)
            c.inc(v.tensor_tensor(comb, oh1, pw[:, 0, :].unsqueeze(2).to_broadcast([P, NB, NX]), ALU.mult))
            c.inc(v.tensor_tensor(cum, oh2, pw[:, 1, :].unsqueeze(2).to_broadcast([P, NB, NX]), ALU.mult))
            c.wait(v)
            v.tensor_tensor(comb, comb, cum, ALU.add).then_inc(s_comb, 1)
            v.wait_ge(s_cnt, 1)
            v.wait_ge(s_comb, 1)
            tot = tok(ps[:, 7, 0:NB * NX])
            within = tok(ps[:, 6, 0:NB * NX])
            c.inc(v.tensor_copy(gt, tot))
            c.inc(v.memset(excl, 1.0))
            c.wait(v)
            for e in range(NX):
                c.inc(v.tensor_tensor_scan(cum[:, :, e], excl[:, :, e], gt[:, :, e], 0.0, ALU.mult, ALU.add))
            c.wait(v)
            c.inc(v.tensor_tensor(excl, cum, gt, ALU.subtract))
            c.inc(v.tensor_scalar(tl[:, 0, :], cum[:, NB - 1, :], float(P - 1), None, ALU.add))
            c.wait(v)
            c.inc(v.tensor_tensor(excl, excl, within, ALU.add))
            c.inc(v.tensor_copy(tli, tl[:, 0, :]))
            c.wait(v)
            c.inc(v.tensor_scalar(tli, tli, 7, None, ALU.logical_shift_right))
            c.inc(v.memset(tl[:, 4, :], 1.0))
            c.wait(v)
            c.inc(v.tensor_copy(tl[:, 1, :], tli))
            c.wait(v)
            c.inc(v.tensor_tensor_scan(tl[:, 2, :], tl[:, 4, :], tl[:, 1, :], 0.0, ALU.mult, ALU.add))
            c.wait(v)
            c.inc(v.tensor_tensor(tl[:, 3, :], tl[:, 2, :], tl[:, 1, :], ALU.subtract))
            c.wait(v)
            c.inc(v.tensor_scalar(tl[:, 5, :], tl[:, 3, :], float(P), None, ALU.mult))
            c.wait(v)
            c.inc(v.tensor_tensor(excl, excl, tl[:, 5, :].unsqueeze(1).to_broadcast([P, NB, NX]), ALU.add))
            c.wait(v)
            for j, oh in enumerate((oh1, oh2)):
                c.inc(v.tensor_tensor(cum, excl, oh, ALU.mult))
                c.wait(v)
                c.inc(v.tensor_reduce(ms[:, j, :], cum, X, ALU.add))
                c.wait(v)
                c.inc(v.tensor_copy(pos[:, :, j], ms[:, j, :]))
            c.inc(v.memset(etf[:, 0, :], 0.0))
            for e in range(1, NX):
                c.wait(v)
                c.inc(v.tensor_scalar(etf[:, 1, :], iota16[0:1, :], tl[0:1, 3, e:e + 1], None, ALU.is_ge))
                c.wait(v)
                c.inc(v.tensor_tensor(etf[:, 0, :], etf[:, 0, :], etf[:, 1, :], ALU.add))
            c.wait(v)
            v.tensor_copy(etab[:, :], etf[:, 0, :]).then_inc(s_etab, 1)
            c.wait(v)

            def combine(i, slot):
                if late(i):
                    v.wait_ge(s_ct, i - 1)
                v.tensor_scalar(cs[:, slot, :], blk(comb, i), 1.0, None, ALU.mult).then_inc(s_cs, 1)

            combine(0, 0)

            def place_rows(i, slot):
                if not isinstance(i, int) or i < NB - 1:
                    combine(i + 1, 1 - slot)
                if late(i):
                    v.wait_ge(s_sc[slot], both(slot, i - 2) * 2)
                normal(i, slot, s_posx)
                v.wait_ge(s_bp, i + 1)
                if late(i):
                    v.wait_ge(s_x2s[slot], both(slot, i - 2))
                v.tensor_tensor(as3[:, slot, :], blk(x_sb, i), ps[:, 2 + slot, 0:D], ALU.add).then_inc(s_x2b, 1)
            pairs(v, NB, place_rows)

            def turned4(j, slot):
                v.wait_ge(s_xt4, j + 1)
                if late(j):
                    v.wait_ge(s_h1[1], j - 1)
                v.tensor_copy(xsT[:, slot, :], ps[:, slot, 0:D]).then_inc(s_xc, 1)

            def hidden(j, slot):
                e = v.value_load(etab[0:1, bass.ds(j, 1)], min_val=0, max_val=NX - 1)
                v.wait_ge(s_h1[1], j + 1)
                if late(j):
                    v.wait_ge(s_y, j - 1)
                for c4 in range(FC // 2, FC):
                    last = v.tensor_scalar(hT[:, slot, c4, :], ps[:, 3 + 2 * slot, (c4 - FC // 2) * P:(c4 - FC // 2 + 1) * P],
                                           flat(b1[:, bass.ds(e, 1), c4:c4 + 1]), 0.0, ALU.add, ALU.max)
                last.then_inc(s_hd, 1)

            def result(j, slot):
                v.wait_ge(s_y, j + 1)
                if late(j):
                    v.wait_ge(s_yst[slot], both(slot, j - 2))
                v.tensor_copy(ys[:, slot, :], ps[:, 6 + slot, 0:D]).then_inc(s_yc, 1)

            v.wait_ge(s_x2b, NB)
            turned4(0, 0)

            def work4(j, slot):
                if not isinstance(j, int) or j < NT - 1:
                    turned4(j + 1, 1 - slot)
                hidden(j, slot)
                if late(j, 1):
                    result(j - 1, 1 - slot)
            ffn_steps(v, work4)
            result(NT - 1, (NT - 1) % 2)

            def add(i, slot):
                v.wait_ge(s_yg[slot], both(slot, i) * 2)
                v.wait_ge(s_x5[slot], both(slot, i))
                if late(i):
                    v.wait_ge(s_out5[slot], both(slot, i - 2))
                v.scalar_tensor_tensor(o5[:, slot, :], y1[:, slot, :], pw[:, 0, bass.ds(i, 1)], x5[:, slot, :],
                                       ALU.mult, ALU.add).then_inc(s_o1, 1)
                v.wait_ge(s_o1, i + 1)
                v.scalar_tensor_tensor(o5[:, slot, :], y2[:, slot, :], pw[:, 1, bass.ds(i, 1)], o5[:, slot, :],
                                       ALU.mult, ALU.add).then_inc(s_o, 1)
            pairs(v, NB, add)

        def stage4_sync(sp):
            for slot in range(2):
                sp.wait_ge(s_sc[slot], 32 * ((NB + 1 - slot) // 2))
                sp.wait_ge(s_x2s[slot], 16 * ((NB + 1 - slot) // 2))
            sp.wait_ge(s_xz, 16)

            def load(j, slot):
                if late(j):
                    sp.wait_ge(s_h1[1], j - 1)
                e = sp.value_load(etab[0:1, bass.ds(j, 1)], min_val=0, max_val=NX - 1)
                sp.dma_start(w1[:, slot, :, :], a["w1"][bass.ds(e, 1), :, :].rearrange("a (k p) f -> p (a k) f", p=P)
                             ).then_inc(s_w1[slot], 16)
                sp.dma_start(xs[:, slot, :], xs_d[bass.ds(j * P, P), :]).then_inc(s_xs[slot], 16)

            def store(j, slot):
                sp.wait_ge(s_yc, j + 1)
                sp.dma_start(ys_d[bass.ds(j * P, P), :], ys[:, slot, :]).then_inc(s_yst[slot], 16)
            load(0, 0)
            load(1, 1)

            def work4(j, slot):
                if not isinstance(j, int) or j < NT - 2:
                    load(j + 2, slot)
                if late(j, 2):
                    store(j - 2, slot)
            ffn_steps(sp, work4)
            store(NT - 2, (NT - 2) % 2)
            store(NT - 1, (NT - 1) % 2)

            def load5(i, slot):
                if late(i):
                    sp.wait_ge(s_o1, i - 1)
                sp.dma_start(x5[:, slot, :], x2_d[bass.ds(i * P, P), :]).then_inc(s_x5[slot], 16)

            def store5(i, slot):
                sp.wait_ge(s_o, i + 1)
                if isinstance(i, int) and i == NB - 1:
                    sp.dma_start(out[i * P:N, :], o5[0:N - i * P, slot, :]).then_inc(s_out5[slot], 16)
                else:
                    sp.dma_start(out[bass.ds(i * P, P), :], o5[:, slot, :]).then_inc(s_out5[slot], 16)
            load5(0, 0)

            def work5(i, slot):
                if not isinstance(i, int) or i < NB - 1:
                    load5(i + 1, 1 - slot)
                store5(i, slot)
            work5(0, 0)
            work5(1, 1)
            turns = (NB - 3) // 2
            with sp.Fori(0, turns) as t:
                work5(t * 2 + 2, 0)
                work5(t * 2 + 3, 1)
            for i in range(2 + 2 * turns, NB):
                work5(i, i % 2)
            for slot in range(2):
                sp.wait_ge(s_out5[slot], 16 * ((NB + 1 - slot) // 2))

        @block.sync
        def _(sp):
            sync1(sp)
            sync2(sp)
            stage3_sync(sp)
            stage4_sync(sp)

        @block.gpsimd
        def _(pool):
            pool1(pool)
            pool2(pool)
            stage3_pool(pool)

        @block.vector
        def _(v):
            dve1(v)
            dve2(v)
            stage3_dve(v)

        @block.scalar
        def _(act):
            act1(act)
            act2(act)
            stage3_act(act)

        @block.tensor
        def _(pe):
            pe1(pe)
            pe2(pe)
            stage3_pe(pe)


def kernel(x, src, dst, edge_weight, node_vec, **w):
    import numpy as np
    import concourse.bacc as bacc
    from concourse.bass_utils import run_bass_kernel_spmd

    def padded(v, n, fill=0):
        v = np.asarray(v)
        return np.concatenate([v, np.full((n - v.shape[0],) + v.shape[1:], fill, v.dtype)])

    def edge_tiles(v, fill):
        return np.ascontiguousarray(padded(v, EPAD, fill).reshape(NG, GT, P).transpose(0, 2, 1).reshape(NG * P, GT))

    def halves(v):
        return np.ascontiguousarray(np.asarray(v).reshape(2, P).T)
    g = {k: np.asarray(v) for k, v in w.items()}
    f32 = np.float32
    heads = np.arange(D).reshape(2, P) // HD
    arrays = {
        "x": padded(x, NPAD),
        "src": edge_tiles(src, 0),
        "dst": edge_tiles(dst, NPAD),
        "ew": edge_tiles(edge_weight, 0),
        "dst_rows": padded(dst, EPAD, NPAD).reshape(NC // 2, 2, CH),
        "nv": np.ascontiguousarray(padded(node_vec, NPAD).reshape(NB, P).T),
        "wq": g["L0_gnn_Wq"], "bq": g["L0_gnn_bq"], "wk": g["L0_gnn_Wk"], "bk": g["L0_gnn_bk"],
        "wv": g["L0_gnn_Wv"], "bv": g["L0_gnn_bv"], "wt": g["L0_gnn_Wt"].reshape(-1), "bt": g["L0_gnn_bt"],
        "wo": g["L0_gnn_Wo"], "bo": g["L0_gnn_bo"],
        "klw": halves(g["L0_mix_kln_weight"]), "klb": halves(g["L0_mix_kln_bias"]),
        "vlw": g["L0_mix_vln_weight"].reshape(-1), "vlb": g["L0_mix_vln_bias"].reshape(-1),
        "ident": np.eye(P, dtype=f32),
        "headind": (np.arange(H)[:, None, None] == heads[None]).astype(f32),
        "upper": np.triu(np.ones((P, P), f32), 1),
        "wg": np.ascontiguousarray(g["L0_ffn_Wg"].T), "bg": g["L0_ffn_bg"],
        "w1": np.ascontiguousarray(g["L0_ffn_W1"].transpose(0, 2, 1)), "b1": g["L0_ffn_b1"],
        "w2": np.ascontiguousarray(g["L0_ffn_W2"].transpose(0, 2, 1)), "b2": g["L0_ffn_b2"],
        "hmask": (np.arange(P)[:, None] // HD == np.arange(P)[None] // HD).astype(f32),
    }
    nc = bacc.Bacc("TRN2", target_bir_lowering=False, num_devices=1)
    a = {k: nc.dram_tensor("in_" + k, v.shape, mybir.dt.from_np(v.dtype), kind="ExternalInput").ap() for k, v in arrays.items()}
    out = nc.dram_tensor("out", (N, D), F32, kind="ExternalOutput").ap()
    build(nc, a, out)
    return run_bass_kernel_spmd(nc, [{"in_" + k: v for k, v in arrays.items()}], core_ids=[0]).results[0]["out"]
```
